# Optimizing a Trainium2 kernel written in Bass

```python
import numpy as np
import jax
import jax.numpy as jnp

def _softmax(x, axis=-1):
    return jax.nn.softmax(x, axis=axis)

def _gelu(x):
    return jax.nn.gelu(x, approximate=True)

def _silu(x):
    return jax.nn.silu(x)

def _sigmoid(x):
    return jax.nn.sigmoid(x)

def _layernorm(x, axis=-1, eps=1e-05):
    m = jnp.mean(x, axis=axis, keepdims=True)
    v = jnp.var(x, axis=axis, keepdims=True)
    return (x - m) / jnp.sqrt(v + eps)

def _scatter_add(tgt, idx, src, axis=0):
    return tgt.at[idx].add(src)

def _segment_sum(src, seg, n):
    return jax.ops.segment_sum(src, seg, n)
kernel_name = 'mk_dlrm_tower_d1_rec_r8_bd6c0c'

def setup_inputs(seed: int=0):
    np.random.seed(seed)
    _w = jnp.asarray

    def _rec_inputs():
        import jax
        import jax.numpy as jnp
        _tk = jax.random.key(seed)
        dense_ctx = jax.random.normal(jax.random.fold_in(_tk, 190), (2048, 16), jnp.float32)
        ids = jnp.stack([jax.random.randint(jax.random.fold_in(_tk, 200 + f), (2048,), 0, v, jnp.int32) for f, v in enumerate([1250, 125000, 125000, 1000, 1250, 12500, 12500, 12500, 1250, 1250, 12500, 125000, 1250, 1000, 1250, 1250, 125000, 1000, 1250, 12500, 12500, 1000, 12500, 12500, 1000, 1250, 1000, 12500, 12500, 1250, 12500, 1000, 125000, 1250, 1000, 1000, 1250, 1250, 1250, 1000])], axis=1)
        tbl_0 = 0.05 * jax.random.normal(jax.random.fold_in(_tk, 500 + 0), (1250, 32), jnp.float32)
        tbl_1 = 0.05 * jax.random.normal(jax.random.fold_in(_tk, 500 + 1), (125000, 32), jnp.float32)
        tbl_2 = 0.05 * jax.random.normal(jax.random.fold_in(_tk, 500 + 2), (125000, 32), jnp.float32)
        tbl_3 = 0.05 * jax.random.normal(jax.random.fold_in(_tk, 500 + 3), (1000, 32), jnp.float32)
        tbl_4 = 0.05 * jax.random.normal(jax.random.fold_in(_tk, 500 + 4), (1250, 32), jnp.float32)
        tbl_5 = 0.05 * jax.random.normal(jax.random.fold_in(_tk, 500 + 5), (12500, 32), jnp.float32)
        tbl_6 = 0.05 * jax.random.normal(jax.random.fold_in(_tk, 500 + 6), (12500, 32), jnp.float32)
        tbl_7 = 0.05 * jax.random.normal(jax.random.fold_in(_tk, 500 + 7), (12500, 32), jnp.float32)
        tbl_8 = 0.05 * jax.random.normal(jax.random.fold_in(_tk, 500 + 8), (1250, 32), jnp.float32)
        tbl_9 = 0.05 * jax.random.normal(jax.random.fold_in(_tk, 500 + 9), (1250, 32), jnp.float32)
        tbl_10 = 0.05 * jax.random.normal(jax.random.fold_in(_tk, 500 + 10), (12500, 32), jnp.float32)
        tbl_11 = 0.05 * jax.random.normal(jax.random.fold_in(_tk, 500 + 11), (125000, 32), jnp.float32)
        tbl_12 = 0.05 * jax.random.normal(jax.random.fold_in(_tk, 500 + 12), (1250, 32), jnp.float32)
        tbl_13 = 0.05 * jax.random.normal(jax.random.fold_in(_tk, 500 + 13), (1000, 32), jnp.float32)
        tbl_14 = 0.05 * jax.random.normal(jax.random.fold_in(_tk, 500 + 14), (1250, 32), jnp.float32)
        tbl_15 = 0.05 * jax.random.normal(jax.random.fold_in(_tk, 500 + 15), (1250, 32), jnp.float32)
        tbl_16 = 0.05 * jax.random.normal(jax.random.fold_in(_tk, 500 + 16), (125000, 32), jnp.float32)
        tbl_17 = 0.05 * jax.random.normal(jax.random.fold_in(_tk, 500 + 17), (1000, 32), jnp.float32)
        tbl_18 = 0.05 * jax.random.normal(jax.random.fold_in(_tk, 500 + 18), (1250, 32), jnp.float32)
        tbl_19 = 0.05 * jax.random.normal(jax.random.fold_in(_tk, 500 + 19), (12500, 32), jnp.float32)
        tbl_20 = 0.05 * jax.random.normal(jax.random.fold_in(_tk, 500 + 20), (12500, 32), jnp.float32)
        tbl_21 = 0.05 * jax.random.normal(jax.random.fold_in(_tk, 500 + 21), (1000, 32), jnp.float32)
        tbl_22 = 0.05 * jax.random.normal(jax.random.fold_in(_tk, 500 + 22), (12500, 32), jnp.float32)
        tbl_23 = 0.05 * jax.random.normal(jax.random.fold_in(_tk, 500 + 23), (12500, 32), jnp.float32)
        tbl_24 = 0.05 * jax.random.normal(jax.random.fold_in(_tk, 500 + 24), (1000, 32), jnp.float32)
        tbl_25 = 0.05 * jax.random.normal(jax.random.fold_in(_tk, 500 + 25), (1250, 32), jnp.float32)
        tbl_26 = 0.05 * jax.random.normal(jax.random.fold_in(_tk, 500 + 26), (1000, 32), jnp.float32)
        tbl_27 = 0.05 * jax.random.normal(jax.random.fold_in(_tk, 500 + 27), (12500, 32), jnp.float32)
        tbl_28 = 0.05 * jax.random.normal(jax.random.fold_in(_tk, 500 + 28), (12500, 32), jnp.float32)
        tbl_29 = 0.05 * jax.random.normal(jax.random.fold_in(_tk, 500 + 29), (1250, 32), jnp.float32)
        tbl_30 = 0.05 * jax.random.normal(jax.random.fold_in(_tk, 500 + 30), (12500, 32), jnp.float32)
        tbl_31 = 0.05 * jax.random.normal(jax.random.fold_in(_tk, 500 + 31), (1000, 32), jnp.float32)
        tbl_32 = 0.05 * jax.random.normal(jax.random.fold_in(_tk, 500 + 32), (125000, 32), jnp.float32)
        tbl_33 = 0.05 * jax.random.normal(jax.random.fold_in(_tk, 500 + 33), (1250, 32), jnp.float32)
        tbl_34 = 0.05 * jax.random.normal(jax.random.fold_in(_tk, 500 + 34), (1000, 32), jnp.float32)
        tbl_35 = 0.05 * jax.random.normal(jax.random.fold_in(_tk, 500 + 35), (1000, 32), jnp.float32)
        tbl_36 = 0.05 * jax.random.normal(jax.random.fold_in(_tk, 500 + 36), (1250, 32), jnp.float32)
        tbl_37 = 0.05 * jax.random.normal(jax.random.fold_in(_tk, 500 + 37), (1250, 32), jnp.float32)
        tbl_38 = 0.05 * jax.random.normal(jax.random.fold_in(_tk, 500 + 38), (1250, 32), jnp.float32)
        tbl_39 = 0.05 * jax.random.normal(jax.random.fold_in(_tk, 500 + 39), (1000, 32), jnp.float32)
        _rk = jax.random.fold_in(_tk, 7)
        W_top1 = 0.0354441 * jax.random.normal(jax.random.fold_in(_tk, 801), (796, 512), jnp.float32)
        W_top2 = 0.0441942 * jax.random.normal(jax.random.fold_in(_tk, 802), (512, 256), jnp.float32)
        W_top3 = 0.0625 * jax.random.normal(jax.random.fold_in(_tk, 803), (256, 1), jnp.float32)
        b_top1 = jnp.zeros((512,), jnp.float32)
        b_top2 = jnp.zeros((256,), jnp.float32)
        return (dense_ctx, ids, tbl_0, tbl_1, tbl_2, tbl_3, tbl_4, tbl_5, tbl_6, tbl_7, tbl_8, tbl_9, tbl_10, tbl_11, tbl_12, tbl_13, tbl_14, tbl_15, tbl_16, tbl_17, tbl_18, tbl_19, tbl_20, tbl_21, tbl_22, tbl_23, tbl_24, tbl_25, tbl_26, tbl_27, tbl_28, tbl_29, tbl_30, tbl_31, tbl_32, tbl_33, tbl_34, tbl_35, tbl_36, tbl_37, tbl_38, tbl_39, W_top1, b_top1, W_top2, b_top2, W_top3)
    dense_ctx, ids, tbl_0, tbl_1, tbl_2, tbl_3, tbl_4, tbl_5, tbl_6, tbl_7, tbl_8, tbl_9, tbl_10, tbl_11, tbl_12, tbl_13, tbl_14, tbl_15, tbl_16, tbl_17, tbl_18, tbl_19, tbl_20, tbl_21, tbl_22, tbl_23, tbl_24, tbl_25, tbl_26, tbl_27, tbl_28, tbl_29, tbl_30, tbl_31, tbl_32, tbl_33, tbl_34, tbl_35, tbl_36, tbl_37, tbl_38, tbl_39, W_top1, b_top1, W_top2, b_top2, W_top3 = _rec_inputs()

    def _L0_rec_setup():
        import itertools
        import jax, jax.numpy as jnp
        import numpy as np
        B, F, D = (512, 40, 32)
        P = F * (F - 1) // 2

        def _pair_indices(num_fields):
            pairs = np.array(list(itertools.combinations(range(num_fields), 2)), dtype=np.int32)
            return (pairs[:, 0], pairs[:, 1])
        key = jax.random.key(seed)
        k1, k2 = jax.random.split(key)
        x = jax.random.normal(k1, (B, F, D), dtype=jnp.float32)
        W = jax.random.normal(k2, (P, D, D), dtype=jnp.float32) * 0.05
        return {'x': x, 'W': W}
    _L0_rec_all = _L0_rec_setup()
    _L0_rec_in = {k: v for k, v in _L0_rec_all.items() if k in ('W',)}
    del _L0_rec_all
    return {'dense_ctx': dense_ctx, 'ids': ids, 'tbl_0': tbl_0, 'tbl_1': tbl_1, 'tbl_2': tbl_2, 'tbl_3': tbl_3, 'tbl_4': tbl_4, 'tbl_5': tbl_5, 'tbl_6': tbl_6, 'tbl_7': tbl_7, 'tbl_8': tbl_8, 'tbl_9': tbl_9, 'tbl_10': tbl_10, 'tbl_11': tbl_11, 'tbl_12': tbl_12, 'tbl_13': tbl_13, 'tbl_14': tbl_14, 'tbl_15': tbl_15, 'tbl_16': tbl_16, 'tbl_17': tbl_17, 'tbl_18': tbl_18, 'tbl_19': tbl_19, 'tbl_20': tbl_20, 'tbl_21': tbl_21, 'tbl_22': tbl_22, 'tbl_23': tbl_23, 'tbl_24': tbl_24, 'tbl_25': tbl_25, 'tbl_26': tbl_26, 'tbl_27': tbl_27, 'tbl_28': tbl_28, 'tbl_29': tbl_29, 'tbl_30': tbl_30, 'tbl_31': tbl_31, 'tbl_32': tbl_32, 'tbl_33': tbl_33, 'tbl_34': tbl_34, 'tbl_35': tbl_35, 'tbl_36': tbl_36, 'tbl_37': tbl_37, 'tbl_38': tbl_38, 'tbl_39': tbl_39, 'W_top1': W_top1, 'b_top1': b_top1, 'W_top2': W_top2, 'b_top2': b_top2, 'W_top3': W_top3, 'L0_rec_W': _L0_rec_in['W']}

def reference(dense_ctx, ids, tbl_0, tbl_1, tbl_2, tbl_3, tbl_4, tbl_5, tbl_6, tbl_7, tbl_8, tbl_9, tbl_10, tbl_11, tbl_12, tbl_13, tbl_14, tbl_15, tbl_16, tbl_17, tbl_18, tbl_19, tbl_20, tbl_21, tbl_22, tbl_23, tbl_24, tbl_25, tbl_26, tbl_27, tbl_28, tbl_29, tbl_30, tbl_31, tbl_32, tbl_33, tbl_34, tbl_35, tbl_36, tbl_37, tbl_38, tbl_39, W_top1, b_top1, W_top2, b_top2, W_top3, L0_rec_W):
    import jax
    import jax.numpy as jnp

    def _L0_rec_ref(x, W):
        import itertools
        import jax, jax.numpy as jnp
        import numpy as np
        B, F, D = (512, 40, 32)
        P = F * (F - 1) // 2

        def _pair_indices(num_fields):
            pairs = np.array(list(itertools.combinations(range(num_fields), 2)), dtype=np.int32)
            return (pairs[:, 0], pairs[:, 1])
        fi, fj = _pair_indices(x.shape[1])
        S = W + jnp.swapaxes(W, 1, 2)
        xi = x[:, fi, :]
        xj = x[:, fj, :]
        out = jnp.einsum('bpd,pde,bpe->bp', xi, S, xj)
        return out
    e = jnp.stack([tbl_0[ids[:, 0]], tbl_1[ids[:, 1]], tbl_2[ids[:, 2]], tbl_3[ids[:, 3]], tbl_4[ids[:, 4]], tbl_5[ids[:, 5]], tbl_6[ids[:, 6]], tbl_7[ids[:, 7]], tbl_8[ids[:, 8]], tbl_9[ids[:, 9]], tbl_10[ids[:, 10]], tbl_11[ids[:, 11]], tbl_12[ids[:, 12]], tbl_13[ids[:, 13]], tbl_14[ids[:, 14]], tbl_15[ids[:, 15]], tbl_16[ids[:, 16]], tbl_17[ids[:, 17]], tbl_18[ids[:, 18]], tbl_19[ids[:, 19]], tbl_20[ids[:, 20]], tbl_21[ids[:, 21]], tbl_22[ids[:, 22]], tbl_23[ids[:, 23]], tbl_24[ids[:, 24]], tbl_25[ids[:, 25]], tbl_26[ids[:, 26]], tbl_27[ids[:, 27]], tbl_28[ids[:, 28]], tbl_29[ids[:, 29]], tbl_30[ids[:, 30]], tbl_31[ids[:, 31]], tbl_32[ids[:, 32]], tbl_33[ids[:, 33]], tbl_34[ids[:, 34]], tbl_35[ids[:, 35]], tbl_36[ids[:, 36]], tbl_37[ids[:, 37]], tbl_38[ids[:, 38]], tbl_39[ids[:, 39]]], axis=1)
    z = _L0_rec_ref(e, L0_rec_W)
    z = z.reshape(z.shape[0], -1)
    h = jnp.concatenate([z, dense_ctx], axis=1)
    h = jnp.maximum(h @ W_top1 + b_top1, 0.0)
    h = jnp.maximum(h @ W_top2 + b_top2, 0.0)
    y = h @ W_top3
    return y

_drawn_inputs = setup_inputs


def setup_inputs(seed=0):
    import zlib

    import numpy as np

    out = dict(_drawn_inputs(seed))
    spreads = {'b_top1': (0.0, 0.1), 'b_top2': (0.0, 0.1)}
    factors = {'tbl_0': 8.0,
     'tbl_1': 8.0,
     'tbl_2': 8.0,
     'tbl_3': 7.489,
     'tbl_4': 8.0,
     'tbl_5': 7.723,
     'tbl_6': 8.0,
     'tbl_7': 7.93,
     'tbl_8': 7.642,
     'tbl_9': 7.384,
     'tbl_10': 7.872,
     'tbl_11': 8.0,
     'tbl_12': 7.153,
     'tbl_13': 7.73,
     'tbl_14': 7.981,
     'tbl_15': 8.0,
     'tbl_16': 8.0,
     'tbl_17': 7.898,
     'tbl_18': 8.0,
     'tbl_19': 8.0,
     'tbl_20': 7.61,
     'tbl_21': 7.973,
     'tbl_22': 8.0,
     'tbl_23': 7.228,
     'tbl_24': 8.0,
     'tbl_25': 8.0,
     'tbl_26': 7.844,
     'tbl_27': 8.0,
     'tbl_28': 8.0,
     'tbl_29': 7.935,
     'tbl_30': 7.918,
     'tbl_31': 7.229,
     'tbl_32': 8.0,
     'tbl_33': 8.0,
     'tbl_34': 8.0,
     'tbl_35': 7.444,
     'tbl_36': 8.0,
     'tbl_37': 8.0,
     'tbl_38': 8.0,
     'tbl_39': 7.619}
    for name, (base, spread) in spreads.items():
        noise = np.random.default_rng([zlib.crc32(name.encode()), seed]).standard_normal(out[name].shape)
        drawn = base * np.exp(spread * noise) if base else spread * noise
        out[name] = jnp.asarray(drawn.astype(out[name].dtype))
    for name, factor in factors.items():
        out[name] = (out[name] * factor).astype(out[name].dtype)
    return out
```

```python
from contextlib import ExitStack

import numpy as np

import concourse.bass as bass
from concourse import mybir

B, F, D = 2048, 40, 32
P = 128
NB = 256
G = B // NB
T = NB // P
FC = P // D
C = F // FC
PARTS = 4
NCTX = 16
N1, N2 = 512, 256
M1, M2 = N1 // P, N2 // P
UNITS = [(ci, cj) for cj in range(C) for ci in range(cj + 1)]
NU = len(UNITS)
START = [c * (c + 1) // 2 for c in range(C + 1)]
UPB = 8
NZ = (NU + 1 + UPB - 1) // UPB
SLOTS = 5
SPLITS = 5
TILES = 2 * C + FC * (NU - C)
CU = TILES // FC
SU = CU // SPLITS
PIECES = M1 + M2 + 1
NS = 16

EXPONENT = 0x7F800000
TINY = 2.0 ** -60
X_EXP, S_EXP = 13, 12

F32, F16, BF16 = mybir.dt.float32, mybir.dt.float16, mybir.dt.bfloat16
I32, U32 = mybir.dt.int32, mybir.dt.uint32
AX = mybir.AxisListType
ALU, ACT = mybir.AluOpType, mybir.ActivationFunctionType

LEAD_M, LEAD_S, LEAD_L, LEAD_T = 7, 6, 4, 3
TURN_AT = {UPB * k + 7: k for k in range(NZ - 1)} | {50: NZ - 1}
UNDO_AT = {UPB * k + 8: k for k in range(NZ - 1)} | {51: NZ - 1}
Z_OUT_AT = {UPB * k + 10: k for k in range(NZ - 1)}
LATE = 2
CTX_AT = 4
DENSE_FROM = {3: (3, 2, 2), 6: (3, 2, 2), 9: (3, 2, 2), 12: (3, 2, 2),
              16: (1,) * 4, 20: (1,) * 4, 25: (1,) * 2}
HEAD_AT = 22
Y_READ_AT = 30
SPLIT_AT = {-6: 0, -5: 1, 1: 2, 7: 3, 18: 4}

DENSE_AT = {}
for _i, (_at, _counts) in enumerate(DENSE_FROM.items()):
    for _n, _count in enumerate(_counts):
        DENSE_AT[_at + _n] = [(_i, sum(_counts[:_n]) + _m) for _m in range(_count)]


def dense_ks(i):
    return NZ if i < M1 else M1 if i < M1 + M2 else M2


def tile_of(u, q):
    ci, cj = UNITS[u]
    full = u - cj
    return 2 * cj + q if ci == cj else 2 * C + FC * full + q


def split_of(u):
    return tile_of(u, 0) // (FC * SU)


def fields_of(u, q, s):
    ci, cj = UNITS[u]
    if ci == cj:
        return FC * cj + (s + 1 + q) % FC, FC * cj + s
    return FC * ci + q, FC * cj + s


def n_tiles(u):
    return 2 if UNITS[u][0] == UNITS[u][1] else FC


EARLY = sum(START[c] < LEAD_T for c in range(C))


def chunks_at(p, lead):
    own = [(c, False) for c in range(C) if START[c] - lead == p]
    nxt = [(c, True) for c in range(C) if START[c] - lead + NU == p]
    return own + nxt


def bank_x_steps(p, last=False):
    steps = [("chunk", c, nxt) for c, nxt in chunks_at(p, LEAD_T) if not (nxt and last)]
    steps += [("turn", TURN_AT[p], False)] if p in TURN_AT else []
    steps += [("undo", UNDO_AT[p], False)] if p in UNDO_AT else []
    return steps


USES = sum(len(bank_x_steps(p)) for p in range(NU))


def bank_x_uses(g):
    return g * USES + EARLY


def undo_use(k, last):
    steps = [step for p in range(NU) for step in bank_x_steps(p, last)]
    return steps.index(("undo", k, False)) + 1


def y_tiles(p):
    return slice(FC - n_tiles(p), FC) if p == 0 else slice(0, n_tiles(p))


def build(nc, ids, ctx, w, wt, w1, b1, w2, b2, w3, sel, selc, sel_undo, undo_rows, eyef, tables, out):
    with ExitStack() as stack:
        def sb(name, shape, dt):
            return stack.enter_context(nc.sbuf_tensor(name, shape, dt))

        def ps(name, shape, dt):
            return stack.enter_context(nc.psum_tensor(name, shape, dt))

        def sem(name):
            return stack.enter_context(nc.semaphore(name))

        s_parts = sb("s_parts", [P, TILES, P], F16)
        w_sum = sb("w_sum", [P, CU, P], F32)
        w_swapped = sb("w_swapped", [P, CU, P], F32)
        s_h = sb("s_h", [P, 2, SU, P], F16)
        s_l = sb("s_l", [P, 2, SU, P], F16)
        w_max = sb("w_max", [P, SPLITS + 1], F32)
        w_max_all = sb("w_max_all", [1, 3], F32)
        ones = sb("ones", [1, P], F32)
        s_power = sb("s_power", [P, 1], F32)
        s_scale = sb("s_scale", [P, 1], F32)
        undo_rows_s = sb("undo_rows_s", [NS, 2], F32)
        undo_scale = sb("undo_scale", [NS, 1], F32)
        sel_undo_f = sb("sel_undo_f", [NS, NZ, P], F32)
        sel_undo_s = sb("sel_undo_s", [NS, NZ, P], BF16)
        x_max = sb("x_max", [P, 2, T], F32)
        x_power = sb("x_power", [P, T, NS], F32)
        x_scale = sb("x_scale", [P, 2, T], F32)
        powers_t = sb("powers_t", [NS, NB], BF16)
        undo = sb("undo", [P, 2, NB], F32)
        idx = sb("idx", [P, C, T * FC], I32)
        rows = sb("rows", [P, C, T, P + 1], F32)
        parts = sb("parts", [P, 2, T, FC, PARTS, D], F16)
        x_stack = sb("x_stack", [P, F, NB], F16)
        x_chunk = sb("x_chunk", [P, SLOTS, NB], F32)
        prod = sb("prod", [P, 3, FC, NB], F32)
        z = sb("z", [P, NZ, NB], F32)
        z_head = sb("z_head", [P, NB], F32)
        ctx_t = sb("ctx_t", [P, NB], F32)
        w1_s = sb("w1_s", [P, NZ, N1], F32)
        w2_s = sb("w2_s", [P, M1, N2], F32)
        w3_s = sb("w3_s", [P, M2], F32)
        b1_s = sb("b1_s", [P, M1], F32)
        b2_s = sb("b2_s", [P, M2], F32)
        h1 = sb("h1", [P, M1, NB], F32)
        h2 = sb("h2", [P, M2, NB], F32)
        y_s = sb("y_s", [1, NB], F32)
        sel_s = sb("sel_s", [P, UPB, D], F32)
        selc_s = sb("selc_s", [P, FC, D], F32)
        eye_f = sb("eye_f", [P, P], F32)
        eye_h = sb("eye_h", [P, P], F16)
        eye_b = sb("eye_b", [P, P], BF16)

        p_y = ps("p_y", [P, 2, FC, NB], F32)
        p_stack = ps("p_stack", [P, FC, NB], F16)
        p_x = ps("p_x", [P, 512], F32)
        p_d = ps("p_d", [P, 512], F32)
        p_z = ps("p_z", [P, 512], F32)

        ids_ready = [sem(f"ids_ready{c}") for c in range(C)]
        gathered = [sem(f"gathered{c}") for c in range(C)]
        chunk_begun = sem("chunk_begun")
        consts = sem("consts")
        mlp_weights = sem("mlp_weights")
        w_loaded = [sem(f"w_loaded{k}") for k in range(SPLITS)]
        wt_loaded = [sem(f"wt_loaded{k}") for k in range(SPLITS)]
        w_maxed, w_turned, w_power_known, s_power_out, s_scaled = (
            sem(n) for n in ("w_maxed", "w_turned", "w_power_known", "s_power_out", "s_scaled"))
        s_summed, s_high, s_low = (sem(n) for n in ("s_summed", "s_high", "s_low"))
        vector_step = sem("vector_step")
        s_placed = [sem(f"s_placed{k}") for k in range(SPLITS)]
        zeroed = sem("zeroed")
        eye_cast = sem("eye_cast")
        x_maxed, x_scaled, x_high, x_low, x_repeated = (
            sem(n) for n in ("x_maxed", "x_scaled", "x_high", "x_low", "x_repeated"))
        x_powered = sem("x_powered")
        turned, undo_made, undo_cast = (sem(n) for n in ("turned", "undo_made", "undo_cast"))
        transposed = sem("transposed")
        stack_ready = sem("stack_ready")
        bank_x_read = sem("bank_x_read")
        piece_read = sem("piece_read")
        y_ready = sem("y_ready")
        multiplied = sem("multiplied")
        reduced = sem("reduced")
        ctx_added = sem("ctx_added")
        z_copied = sem("z_copied")
        head_moved = sem("head_moved")
        ctx_loaded = sem("ctx_loaded")
        piece_done = sem("piece_done")
        y_stored = sem("y_stored")

        block = stack.enter_context(nc.Block())
        N_PLACED = 16 * PARTS * FC

        def gather_group(pool, g, first):
            for c in range(C):
                pool.wait_ge(ids_ready[c], g * 16 + 16)
                if not first:
                    pool.wait_ge(transposed, g * C + (c - C + 1))
                pool.sem_inc(chunk_begun, 1)
                for t in range(T):
                    for f in range(FC):
                        k = t * FC + f
                        pool.indirect_dma_start(
                            out=rows[:, c, t, f * D:(f + 1) * D], out_offset=None,
                            in_=tables[FC * c + f],
                            in_offset=bass.IndirectOffsetOnAxis(ap=idx[:, c, k:k + 1], axis=0),
                        ).then_inc(gathered[c], 16)

        N_GATHERED = 16 * T * FC

        @block.gpsimd
        def _(pool):
            gather_group(pool, 0, True)
            with pool.Fori(1, G) as g:
                gather_group(pool, g, False)

        @block.sync
        def _(sp):
            for c in range(C):
                sp.dma_start(idx[:, c, :], ids[:, 0, c, :]).then_inc(ids_ready[c], 16)

            def place(k):
                for q in range(FC):
                    for row, src in enumerate((s_h, s_h, s_l, s_l)):
                        tiles = s_parts[D * row:D * row + D, FC * SU * k:FC * SU * (k + 1), :]
                        sp.dma_start(tiles.rearrange("p (u q) n -> p u q n", q=FC)[:, :, q, :],
                                     src[D * q:D * q + D, k % 2, :, :]).then_inc(s_placed[k], 16)

            def reload_ids(g, c):
                sp.wait_ge(gathered[c], g * N_GATHERED + N_GATHERED)
                sp.dma_start(idx[:, c, :], ids[:, bass.ds(g + 1, 1), c, :].rearrange("p a k -> p (a k)")).then_inc(ids_ready[c], 16)

            for k in range(SPLITS):
                sp.dma_start(w_sum[:, k * SU:(k + 1) * SU, :],
                             w[:, k * SU:(k + 1) * SU, :]).then_inc(w_loaded[k], 16)
            sp.dma_start(eye_f[:, :], eyef).then_inc(consts, 16)
            sp.dma_start(sel_s[:, :, :], sel).then_inc(consts, 16)
            sp.dma_start(selc_s[:, :, :], selc).then_inc(consts, 16)
            sp.dma_start(sel_undo_f[:, :, :], sel_undo).then_inc(consts, 16)
            sp.dma_start(undo_rows_s[:, :], undo_rows).then_inc(consts, 16)
            for k in range(SPLITS):
                sp.dma_start(w_swapped[:, k * SU:(k + 1) * SU, :],
                             wt[:, k * SU:(k + 1) * SU, :]).then_inc(wt_loaded[k], 16)
            for k in range(SPLITS):
                if k == SPLITS - 1:
                    for c in range(C // 2):
                        reload_ids(0, c)
                sp.wait_ge(s_low, k + 1)
                place(k)
            sp.dma_start(w1_s[:, :, :], w1).then_inc(mlp_weights, 16)
            sp.dma_start(w2_s[:, :, :], w2).then_inc(mlp_weights, 16)
            sp.dma_start(w3_s[:, :], w3).then_inc(mlp_weights, 16)
            sp.dma_start(b1_s[:, :], b1).then_inc(mlp_weights, 16)
            sp.dma_start(b2_s[:, :], b2).then_inc(mlp_weights, 16)
            for c in range(C // 2, C):
                reload_ids(0, c)

            with sp.Fori(1, G - 1) as g:
                for c in range(C):
                    reload_ids(g, c)

        steps = [0]

        def in_turn(v, instruction):
            steps[0] += 1
            instruction.then_inc(vector_step, 1)
            v.wait_ge(vector_step, steps[0])

        def s_scale_step(v):
            for k in range(SPLITS):
                v.wait_ge(w_loaded[k], 16)
                in_turn(v, nc.vector.tensor_reduce(w_max[:, k:k + 1],
                                                   w_sum[:, k * SU:(k + 1) * SU, :].rearrange("p t n -> p (t n)"),
                                                   AX.X, ALU.max, apply_absolute_value=True))
            nc.vector.tensor_reduce(w_max[:, SPLITS:SPLITS + 1], w_max[:, 0:SPLITS], AX.X,
                                    ALU.max).then_inc(w_maxed, 1)
            v.wait_ge(w_turned, 1)
            in_turn(v, nc.vector.tensor_reduce(w_max_all[:, 0:1], p_d[0:1, 0:P], AX.X, ALU.max))
            in_turn(v, nc.vector.tensor_scalar(w_max_all[:, 1:2], w_max_all[:, 0:1], TINY, None, ALU.max))
            nc.vector.tensor_scalar(w_max_all[:, 2:3].bitcast(I32), w_max_all[:, 1:2].bitcast(I32),
                                    EXPONENT, None, ALU.bitwise_and).then_inc(w_power_known, 1)
            v.wait_ge(s_power_out, 1)
            in_turn(v, nc.vector.tensor_copy(s_power[:, :], p_d[:, 256:257]))
            nc.vector.tensor_scalar(s_scale[:, :].bitcast(I32), s_power[:, :].bitcast(I32), -1.0,
                                    float((254 + S_EXP) << 23), ALU.mult, ALU.add).then_inc(s_scaled, 1)
            v.wait_ge(consts, 16 * 5)
            in_turn(v, nc.vector.scalar_tensor_tensor(undo_scale[:, :], undo_rows_s[:, 0:1], s_power[0:NS, 0:1],
                                                      undo_rows_s[:, 1:2], ALU.mult, ALU.add))
            nc.vector.tensor_scalar(sel_undo_s[:, :, :], sel_undo_f[:, :, :], undo_scale[:, 0:1], None,
                                    ALU.mult).then_inc(undo_cast, 1)

        def split_s_vector(v, k):
            piece = slice(k * SU, (k + 1) * SU)
            v.wait_ge(wt_loaded[k], 16)
            nc.vector.tensor_tensor(w_sum[:, piece, :], w_sum[:, piece, :], w_swapped[:, piece, :],
                                    ALU.add).then_inc(s_summed, 1)
            v.wait_ge(s_high, k + 1)
            if k >= 2:
                v.wait_ge(s_placed[k - 2], N_PLACED)
            nc.vector.scalar_tensor_tensor(
                s_l[:, k % 2, :, :].rearrange("p t n -> p (t n)"),
                w_sum[:, piece, :].rearrange("p t n -> p (t n)"), s_scale[:, 0:1],
                s_h[:, k % 2, :, :].rearrange("p t n -> p (t n)"), ALU.mult, ALU.subtract).then_inc(s_low, 1)

        def x_max_step(v, g, n, c, young):
            v.wait_ge(gathered[c], g * N_GATHERED + N_GATHERED)
            if not (young and c < 2):
                v.wait_ge(x_powered, n - 1)
            nc.vector.tensor_reduce(x_max[:, c % 2, :], rows[:, c, :, :], AX.X, ALU.max,
                                    apply_absolute_value=True).then_inc(x_maxed, 1)

        def x_power_step(v, n, c, turns):
            v.wait_ge(x_maxed, n + 1)
            if turns is not None:
                v.wait_ge(turned, turns)
            nc.vector.tensor_scalar(x_power[:, :, c].bitcast(I32), x_max[:, c % 2, :].bitcast(I32),
                                    EXPONENT, None, ALU.bitwise_and).then_inc(x_powered, 1)

        def x_scale_step(v, n, c, young):
            v.wait_ge(x_powered, n + 1)
            if not (young and c < 2):
                v.wait_ge(x_low, n - 1)
            nc.vector.tensor_scalar(x_scale[:, c % 2, :].bitcast(I32), x_power[:, :, c].bitcast(I32), -1.0,
                                    float((254 + X_EXP) << 23), ALU.mult, ALU.add).then_inc(x_scaled, 1)

        def x_low_step(v, n, c):
            v.wait_ge(x_high, n + 1)
            for t in range(T):
                last = nc.vector.scalar_tensor_tensor(
                    parts[:, c % 2, t, :, 1, :], rows[:, c, t, 0:P].rearrange("p (f d) -> p f d", f=FC),
                    x_scale[:, c % 2, t:t + 1], parts[:, c % 2, t, :, 0, :], ALU.mult, ALU.subtract)
            last.then_inc(x_low, 1)

        def z_out(v, g, k, young, last):
            v.wait_ge(bank_x_read, bank_x_uses(g) + undo_use(k, last))
            if k < NZ - 1:
                v.wait_ge(reduced, g * NU + UPB * (k + 1))
            else:
                v.wait_ge(ctx_added, g + 1)
            if k == 0 and not young:
                v.wait_ge(head_moved, g)
            if k == 1 and not young:
                v.wait_ge(piece_done, g * PIECES - PIECES + M1)
            nc.vector.tensor_tensor(z[:, k, :] if k else z_head[:, :], p_z[:, 0:NB], undo[:, k % 2, :],
                                    ALU.mult).then_inc(z_copied, 1)

        def product(v, g, p, first):
            ci, cj = UNITS[p]
            nt = n_tiles(p)
            if ci == 0:
                v.wait_ge(stack_ready, g * C + (cj + 1))
            v.wait_ge(y_ready, g * NU + (p + 1))
            if p >= 3:
                v.wait_ge(reduced, g * NU + (p - 2))
            elif not first:
                v.wait_ge(reduced, g * NU + (p - 3))
            nc.vector.tensor_tensor(
                prod[:, p % 3, y_tiles(p), :], p_y[:, p % 2, y_tiles(p), :],
                x_chunk[:, cj % SLOTS, :].unsqueeze(1).broadcast_to([P, nt, NB]),
                ALU.mult).then_inc(multiplied, 1)

        def vector_position(v, g, p, first=False, last=False):
            def chunks(lead):
                return [(c, g + 1 if nxt else g, (g + 1 if nxt else g) * C + c, first and not nxt)
                        for c, nxt in chunks_at(p, lead) if not (nxt and last)]
            if first and p in SPLIT_AT:
                split_s_vector(v, SPLIT_AT[p])
            for c, _gg, n, _young in chunks(LEAD_L):
                x_low_step(v, n, c)
            for c, _gg, n, young in chunks(LEAD_S):
                x_scale_step(v, n, c, young)
            for c, gg, n, young in chunks(LEAD_M):
                x_max_step(v, gg, n, c, young)
            if p in Z_OUT_AT:
                z_out(v, g, Z_OUT_AT[p], first, last)
            if p == LATE and not first:
                z_out(v, g - 1, NZ - 1, False, False)
            if p >= 0:
                product(v, g, p, first)
            for c, _gg, n, _young in chunks(LEAD_M):
                k = sum(at < p for at in TURN_AT)
                x_power_step(v, n, c, g * NZ + k if k or not first else None)

        @block.vector
        def _(v):
            nc.vector.memset(ctx_t[:, :], 0.0).then_inc(zeroed, 1)
            nc.vector.memset(x_power[:, :, :], 1.0).then_inc(zeroed, 1)
            nc.vector.memset(ones[:, :], 1.0).then_inc(zeroed, 1)
            nc.vector.memset(rows[:, :, :, P:P + 1], TINY).then_inc(zeroed, 1)
            v.wait_ge(zeroed, 4)
            s_scale_step(v)
            for p in range(-LEAD_M, NU):
                vector_position(v, 0, p, first=True)
            with v.Fori(1, G - 1) as g:
                for p in range(NU):
                    vector_position(v, g, p)
            for p in range(NU):
                vector_position(v, G - 1, p, last=True)
            z_out(v, G - 1, NZ - 1, False, True)

        def split_s_scalar(a, k):
            a.wait_ge(s_summed, k + 1)
            if k == 0:
                a.wait_ge(s_scaled, 1)
            if k >= 2:
                a.wait_ge(s_placed[k - 2], N_PLACED)
            nc.scalar.activation(s_h[:, k % 2, :, :], w_sum[:, k * SU:(k + 1) * SU, :], ACT.Copy,
                                 scale=s_scale[:, 0:1]).then_inc(s_high, 1)

        def x_high_step(a, n, c, young):
            a.wait_ge(x_scaled, n + 1)
            if not (young and c < 2):
                a.wait_ge(transposed, n - 1)
            for t in range(T):
                last = nc.scalar.activation(parts[:, c % 2, t, :, 0, :],
                                            rows[:, c, t, 0:P].rearrange("p (f d) -> p f d", f=FC),
                                            ACT.Copy, scale=x_scale[:, c % 2, t:t + 1])
            last.then_inc(x_high, 1)

        def repeat_parts(a, n, c):
            a.wait_ge(x_low, n + 1)
            pairs = parts[:, c % 2, :, :, :, :].rearrange("p t f a d -> p (t f) (a d)")
            nc.scalar.activation(pairs[:, :, 2 * D:4 * D], pairs[:, :, 0:2 * D], ACT.Copy).then_inc(x_repeated, 1)

        def load_ctx(a, g):
            a.dma_start(ctx_t[0:NCTX, :], ctx[:, bass.ds(g * NB, NB)]).then_inc(ctx_loaded, 16)

        def transposed_out(a, g, n, c, young):
            a.wait_ge(transposed, n + 1)
            if c >= SLOTS:
                a.wait_ge(multiplied, g * NU + START[c - SLOTS + 1])
            elif not young:
                a.wait_ge(multiplied, g * NU - NU + START[c + C - SLOTS + 1])
            nc.scalar.activation(x_chunk[:, c % SLOTS, :], p_x[:, 0:NB], ACT.Copy).then_inc(bank_x_read, 1)
            if not young:
                a.wait_ge(y_ready, g * NU - NU + START[C - 1] + c + 1)
            nc.scalar.activation(x_stack[:, FC * c:FC * (c + 1), :], p_stack[:, :, :],
                                 ACT.Copy).then_inc(stack_ready, 1)

        def powers_out(a, g, k):
            a.wait_ge(turned, g * NZ + (k + 1))
            nc.scalar.activation(powers_t[:, :], p_x[0:NS, 0:NB], ACT.Copy).then_inc(bank_x_read, 1)

        def undo_out(a, g, k, first):
            a.wait_ge(undo_made, g * NZ + (k + 1))
            if k >= 2:
                a.wait_ge(z_copied, g * NZ + (k - 1))
            elif not first:
                a.wait_ge(z_copied, g * NZ)
            nc.scalar.activation(undo[:, k % 2, :], p_x[:, 0:NB], ACT.Copy).then_inc(bank_x_read, 1)

        def piece_out(a, g, i, young):
            a.wait_ge(piece_done, g * PIECES + (i + 1))
            if i < M1:
                nc.scalar.activation(h1[:, i, :], p_d[:, 0:NB], ACT.Relu,
                                     bias=b1_s[:, i:i + 1]).then_inc(piece_read, 1)
            elif i < M1 + M2:
                m = i - M1
                nc.scalar.activation(h2[:, m, :], p_d[:, 0:NB], ACT.Relu,
                                     bias=b2_s[:, m:m + 1]).then_inc(piece_read, 1)
            else:
                if not young:
                    a.wait_ge(y_stored, g * 16)
                nc.scalar.activation(y_s[:, :], p_d[0:1, 0:NB], ACT.Copy).then_inc(piece_read, 1)
                a.wait_ge(piece_read, g * PIECES + PIECES)
                a.dma_start(out[:, bass.ds(g * NB, NB)], y_s[:, :]).then_inc(y_stored, 16)

        def scalar_position(a, g, p, first=False, last=False):
            if first and p in SPLIT_AT:
                split_s_scalar(a, SPLIT_AT[p])
            for kind, i, nxt in bank_x_steps(p, last):
                gg = g + 1 if nxt else g
                if kind == "chunk":
                    repeat_parts(a, gg * C + i, i)
                    transposed_out(a, gg, gg * C + i, i, first and not nxt)
                elif kind == "turn":
                    powers_out(a, g, i)
                elif kind == "undo":
                    undo_out(a, g, i, first)
            if p == HEAD_AT:
                a.wait_ge(z_copied, g * NZ + 1)
                if not first:
                    a.wait_ge(piece_done, g * PIECES - PIECES + M1)
                nc.scalar.activation(z[:, 0, :], z_head[:, :], ACT.Copy).then_inc(head_moved, 1)
            if not first:
                for i, k in DENSE_AT.get(p, []):
                    if k == dense_ks(i) - 1:
                        piece_out(a, g - 1, i, False)
                if p == CTX_AT:
                    a.wait_ge(ctx_added, g)
                    load_ctx(a, g)
            for c, nxt in chunks_at(p, LEAD_S):
                if not (nxt and last):
                    x_high_step(a, (g + 1) * C + c if nxt else g * C + c, c, first and not nxt)

        @block.scalar
        def _(a):
            a.wait_ge(zeroed, 4)
            load_ctx(a, 0)
            a.wait_ge(consts, 16 * 5)
            nc.scalar.activation(eye_b[:, :], eye_f[:, :], ACT.Copy).then_inc(eye_cast, 1)
            nc.scalar.activation(eye_h[:, :], eye_f[:, :], ACT.Copy).then_inc(eye_cast, 1)
            for p in range(-LEAD_S, NU):
                scalar_position(a, 0, p, first=True)
            a.wait_ge(mlp_weights, 16 * 5)
            with a.Fori(1, G - 1) as g:
                for p in range(NU):
                    scalar_position(a, g, p)
            for p in range(NU):
                scalar_position(a, G - 1, p, last=True)
            for i in range(PIECES):
                piece_out(a, G - 1, i, False)
            a.wait_ge(y_stored, 16 * G)

        def transpose_chunk(t, n, c, bank_uses, young):
            t.wait_ge(x_repeated, n + 1)
            if not (young and c == 0):
                t.wait_ge(stack_ready, n)
                t.wait_ge(bank_x_read, bank_uses)
            for s in range(T):
                nc.tensor.transpose(p_x[:, s * P:(s + 1) * P], rows[:, c, s, 0:P], eye_f[:, :])
            for s in range(T):
                for f in range(FC):
                    last = nc.tensor.transpose(p_stack[:, f, s * P:(s + 1) * P],
                                               parts[:, c % 2, s, f, :, :].rearrange("p a d -> p (a d)"),
                                               eye_h[:, :])
            last.then_inc(transposed, 1)

        def turn_powers(t, g, p, bank_uses, last_group):
            done = sum(START[c] - LEAD_M < p for c in range(C))
            early = 0 if last_group else sum(START[c] - LEAD_M + NU < p for c in range(C))
            t.wait_ge(x_powered, g * C + (done + early))
            t.wait_ge(bank_x_read, bank_uses)
            for s in range(T):
                power = x_power[:, s, :].bitcast(BF16)[:, 1:2 * NS:2]
                last = nc.tensor.matmul(p_x[0:NS, s * P:(s + 1) * P], power, eye_b[:, :], start=True, stop=True)
            last.then_inc(turned, 1)

        def lay_out_undo(t, k, bank_uses):
            t.wait_ge(bank_x_read, bank_uses)
            nc.tensor.matmul(p_x[:, 0:NB], sel_undo_s[:, k, :], powers_t[:, :],
                             start=True, stop=True).then_inc(undo_made, 1)

        def interact(t, g, p, first):
            ci, cj = UNITS[p]
            if ci == 0:
                t.wait_ge(stack_ready, g * C + (cj + 1))
            if first and (p == 0 or split_of(p) > max(split_of(u) for u in range(p))):
                t.wait_ge(s_placed[split_of(p)], N_PLACED)
            if p >= 2:
                t.wait_ge(multiplied, g * NU + (p - 1))
            elif not first:
                t.wait_ge(multiplied, g * NU + (p - 2))
            for q in range(n_tiles(p)):
                tile, y = tile_of(p, q), y_tiles(p).start + q
                if ci != cj:
                    x_i = x_stack[:, FC * ci + q, :]
                    last = nc.tensor.matmul(p_y[:, p % 2, y, :], s_parts[:, tile, :], x_i,
                                            start=True, stop=True)
                else:
                    for s in range(FC):
                        x_i = x_stack[:, fields_of(p, q, s)[0], :]
                        last = nc.tensor.matmul(p_y[D * s:D * s + D, p % 2, y, :],
                                                s_parts[:, tile, D * s:D * s + D], x_i, start=True, stop=True)
            last.then_inc(y_ready, 1)

        def reduce(t, g, p, first):
            k, m = p // UPB, p % UPB
            if m == 0 and not (k == 0 and first):
                t.wait_ge(z_copied, g * NZ + k)
            t.wait_ge(multiplied, g * NU + (p + 1))
            for q in range(n_tiles(p)):
                begin = not any(n_tiles(u) > q for u in range(UPB * k, p))
                end = k < NZ - 1 and not any(n_tiles(u) > q for u in range(p + 1, UPB * (k + 1)))
                last = nc.tensor.matmul(p_z[D * q:D * q + D, 0:NB], sel_s[:, m, :],
                                        prod[:, p % 3, y_tiles(p).start + q, :], start=begin, stop=end)
            last.then_inc(reduced, 1)

        def add_ctx(t, g):
            t.wait_ge(ctx_loaded, g * 16 + 16)
            for q in range(FC):
                last = nc.tensor.matmul(p_z[D * q:D * q + D, 0:NB], selc_s[:, q, :], ctx_t[:, :],
                                        start=False, stop=True)
            last.then_inc(ctx_added, 1)

        def dense_product(t, g, i, k):
            if (i, k) == (0, 0):
                t.wait_ge(z_copied, g * NZ + NZ)
                t.wait_ge(head_moved, g + 1)
            elif k == 0:
                t.wait_ge(piece_read, g * PIECES + i)
            begin, end = k == 0, k == dense_ks(i) - 1
            if i < M1:
                last = nc.tensor.matmul(p_d[:, 0:NB], w1_s[:, k, i * P:(i + 1) * P], z[:, k, :],
                                        start=begin, stop=end)
            elif i < M1 + M2:
                m = i - M1
                last = nc.tensor.matmul(p_d[:, 0:NB], w2_s[:, k, m * P:(m + 1) * P], h1[:, k, :],
                                        start=begin, stop=end)
            else:
                last = nc.tensor.matmul(p_d[0:1, 0:NB], w3_s[:, k:k + 1], h2[:, k, :], start=begin, stop=end)
            if end:
                last.then_inc(piece_done, 1)

        def tensor_group(t, g, first=False, last=False):
            uses = bank_x_uses(g)
            for p in range(NU):
                interact(t, g, p, first)
                for kind, i, nxt in bank_x_steps(p, last):
                    if kind == "chunk":
                        transpose_chunk(t, (g + 1) * C + i if nxt else g * C + i, i, uses, False)
                    elif kind == "turn":
                        turn_powers(t, g, p, uses, last)
                    elif kind == "undo":
                        lay_out_undo(t, i, uses)
                    uses = uses + 1
                if not first:
                    for i, k in DENSE_AT.get(p, []):
                        dense_product(t, g - 1, i, k)
                    if p == Y_READ_AT:
                        t.wait_ge(piece_read, g * PIECES)
                if p >= LATE:
                    reduce(t, g, p - LATE, first)
                elif not first:
                    reduce(t, g - 1, p - LATE + NU, False)
                    if p == LATE - 1:
                        add_ctx(t, g - 1)

        @block.tensor
        def _(t):
            t.wait_ge(consts, 16 * 5)
            t.wait_ge(w_maxed, 1)
            nc.tensor.matmul(p_d[0:1, 0:P], w_max[:, SPLITS:SPLITS + 1], eye_f[:, :],
                             start=True, stop=True).then_inc(w_turned, 1)
            t.wait_ge(w_power_known, 1)
            nc.tensor.matmul(p_d[:, 256:257], ones[:, :], w_max_all[:, 2:3],
                             start=True, stop=True).then_inc(s_power_out, 1)
            t.wait_ge(eye_cast, 2)
            t.wait_ge(undo_cast, 1)
            uses = 0
            for p in range(-LEAD_S, 0):
                for _kind, c, _nxt in bank_x_steps(p):
                    transpose_chunk(t, c, c, uses, True)
                    uses += 1
            tensor_group(t, 0, first=True)
            t.wait_ge(mlp_weights, 16 * 5)
            with t.Fori(1, G - 1) as g:
                tensor_group(t, g)
            tensor_group(t, G - 1, last=True)
            for u in range(NU - LATE, NU):
                reduce(t, G - 1, u, False)
            add_ctx(t, G - 1)
            for i in range(PIECES):
                for k in range(dense_ks(i)):
                    dense_product(t, G - 1, i, k)


def _layouts():
    pair_of = {}
    for i in range(F):
        for j in range(i + 1, F):
            pair_of[i, j] = pair_of[j, i] = len(pair_of) // 2
    tile_pairs = np.zeros((TILES, FC), np.int64)
    z_pair = np.full(NZ * P, -1, np.int64)
    seen = set()
    for u in range(NU):
        for q in range(n_tiles(u)):
            for s in range(FC):
                pair = pair_of[fields_of(u, q, s)]
                tile_pairs[tile_of(u, q), s] = pair
                if pair not in seen:
                    seen.add(pair)
                    z_pair[(u // UPB) * P + D * q + FC * (u % UPB) + s] = pair
    for r in range(NCTX):
        z_pair[(NU // UPB) * P + D * (r // FC) + FC * (NU % UPB) + r % FC] = F * (F - 1) // 2 + r
    sel = np.zeros((P, UPB, D), np.float32)
    for s in range(FC):
        for m in range(UPB):
            sel[D * s:D * s + D, m, FC * m + s] = 1
    selc = np.zeros((P, FC, D), np.float32)
    for r in range(NCTX):
        selc[r, r // FC, FC * (NU % UPB) + r % FC] = 1
    sel_undo = np.zeros((NS, NZ, P), np.float32)
    for u in range(NU):
        for q in range(FC):
            first = D * q + FC * (u % UPB)
            sel_undo[UNITS[u][0], u // UPB, first:first + FC] = 1
            sel_undo[C, NU // UPB, D * q + FC * (NU % UPB):D * q + FC * (NU % UPB) + FC] = 1
    undo_rows = np.zeros((NS, 2), np.float32)
    undo_rows[:C, 0] = 2.0 ** -(X_EXP + S_EXP)
    undo_rows[C:, 1] = 1
    return tile_pairs, z_pair, sel, selc, sel_undo, undo_rows


def kernel(**inputs):
    import concourse.bacc as bacc
    from concourse.bass_utils import run_bass_kernel_spmd

    tile_pairs, z_pair, sel, selc, sel_undo, undo_rows = _layouts()
    a = {k: np.asarray(v) for k, v in inputs.items()}
    ids = a["ids"].reshape(G, T, P, C, FC).transpose(2, 0, 3, 1, 4).reshape(P, G, C, T * FC)
    w = a["L0_rec_W"][tile_pairs]
    w = w.reshape(CU, FC, FC, D, D)
    w1 = np.zeros((NZ * P, N1), np.float32)
    w1[z_pair >= 0] = a["W_top1"][z_pair[z_pair >= 0]]
    arrays = {
        "ids_in": ids,
        "ctx_in": a["dense_ctx"].T,
        "w_in": w.transpose(1, 3, 0, 2, 4).reshape(P, CU, P),
        "wt_in": w.transpose(1, 4, 0, 2, 3).reshape(P, CU, P),
        "w1_in": w1.reshape(NZ, P, N1).transpose(1, 0, 2),
        "b1_in": a["b_top1"].reshape(M1, P).T,
        "w2_in": a["W_top2"].reshape(M1, P, N2).transpose(1, 0, 2),
        "b2_in": a["b_top2"].reshape(M2, P).T,
        "w3_in": a["W_top3"].reshape(M2, P).T,
        "sel_in": sel,
        "selc_in": selc,
        "sel_undo_in": sel_undo,
        "undo_rows_in": undo_rows,
        "eye_in": np.eye(P, dtype=np.float32),
    }
    tables = {f"table{f}_in": a[f"tbl_{f}"] for f in range(F)}
    arrays = {k: np.ascontiguousarray(v) for k, v in {**arrays, **tables}.items()}
    nc = bacc.Bacc("TRN2", target_bir_lowering=False, num_devices=1)
    aps = {k: nc.dram_tensor(k, v.shape, mybir.dt.from_np(v.dtype), kind="ExternalInput").ap()
           for k, v in arrays.items()}
    out = nc.dram_tensor("y_out", (1, B), F32, kind="ExternalOutput").ap()
    build(nc, aps["ids_in"], aps["ctx_in"], aps["w_in"], aps["wt_in"], aps["w1_in"], aps["b1_in"],
          aps["w2_in"], aps["b2_in"], aps["w3_in"], aps["sel_in"], aps["selc_in"], aps["sel_undo_in"],
          aps["undo_rows_in"], aps["eye_in"],
          [aps[f"table{f}_in"] for f in range(F)], out)
    r = run_bass_kernel_spmd(nc, [arrays], core_ids=[0])
    return r.results[0]["y_out"].reshape(B, 1)
```

```python
from contextlib import ExitStack

import numpy as np

import concourse.bass as bass
from concourse import mybir

B, F, D = 2048, 40, 32
P = 128
NB = 256
G = B // NB
T = NB // P
FC = P // D
C = F // FC
PARTS = 4
NCTX = 16
N1, N2 = 512, 256
M1, M2 = N1 // P, N2 // P
UNITS = [(ci, cj) for cj in range(C) for ci in range(cj + 1)]
NU = len(UNITS)
START = [c * (c + 1) // 2 for c in range(C + 1)]
UPB = 8
NZ = (NU + 1 + UPB - 1) // UPB
SLOTS = 5
SPLITS = 5
TILES = 2 * C + FC * (NU - C)
CU = TILES // FC
SU = CU // SPLITS
PIECES = M1 + M2 + 1
NS = 16

EXPONENT = 0x7F800000
TINY = 2.0 ** -90
X_EXP, S_EXP = 13, 12

F32, F16, BF16 = mybir.dt.float32, mybir.dt.float16, mybir.dt.bfloat16
I32, U32 = mybir.dt.int32, mybir.dt.uint32
AX = mybir.AxisListType
ALU, ACT = mybir.AluOpType, mybir.ActivationFunctionType

MAX_AT = (-14, -11, -6, -2, 3, 8, 14, 21, 29, 38)
TRANSPOSE_AT = (-6, -4, -2, 3, 7, 13, 19, 26, 34, 43)
MAX_AT_FIRST = (-8, -5, -2, 0) + MAX_AT[4:]
TRANSPOSE_AT_FIRST = (-4, -1, 1, 4) + TRANSPOSE_AT[4:]
H_DELAY, L_DELAY = 1, 3
BEGIN = MAX_AT_FIRST[0]
TURN_AT = {7: 0, 23: 1, 39: 2}
TURNS = len(TURN_AT)
UNDO_AT = {UPB * k + 8: k for k in range(NZ - 1)} | {51: NZ - 1}
Z_OUT_AT = {UPB * k + 10: k for k in range(NZ - 1)}
LATE = 2
CTX_AT = 4
DENSE_FROM = 4
HEADS = 4
HEADS_AT = 38
Y_READ_AT = TAIL_AT = 50
S_SUM_AT = {-8: 0, -6: 1, 2: 2, 8: 3, 14: 4}
S_LOW_AT = {-6: 0, -5: 1, 3: 2, 9: 3, 15: 4}



def dense_ks(i):
    return NZ if i < M1 else M1 if i < M1 + M2 else M2


DENSE_AT = dict(zip((p for p in range(DENSE_FROM, NU)
                     if (p - NU if p >= NU + TRANSPOSE_AT[0] else p) not in TRANSPOSE_AT),
                    ((i, k) for i in range(PIECES) for k in range(dense_ks(i)))))


def tile_of(u, q):
    ci, cj = UNITS[u]
    full = u - cj
    return 2 * cj + q if ci == cj else 2 * C + FC * full + q


def split_of(u):
    return tile_of(u, 0) // (FC * SU)


def fields_of(u, q, s):
    ci, cj = UNITS[u]
    if ci == cj:
        return FC * cj + (s + 1 + q) % FC, FC * cj + s
    return FC * ci + q, FC * cj + s


def n_tiles(u):
    return 2 if UNITS[u][0] == UNITS[u][1] else FC


def chunks_at(p, at, first=False, last=False, delay=0):
    own = {MAX_AT: MAX_AT_FIRST, TRANSPOSE_AT: TRANSPOSE_AT_FIRST}[at] if first else at
    return ([(c, False) for c in range(C) if own[c] + delay == p] +
            [(c, True) for c in range(C) if at[c] + delay + NU == p and not last])


def bank_x_steps(p, first=False, last=False):
    steps = [("chunk", c, nxt) for c, nxt in chunks_at(p, TRANSPOSE_AT, first, last)]
    steps += [("turn", TURN_AT[p], False)] if p in TURN_AT else []
    steps += [("undo", UNDO_AT[p], False)] if p in UNDO_AT else []
    return steps


USES = sum(len(bank_x_steps(p)) for p in range(NU))


def bank_x_uses(g):
    return g * USES + sum(at < 0 for at in TRANSPOSE_AT)


def undo_use(g, k, first, last):
    steps = [step for p in range(BEGIN if first else 0, NU) for step in bank_x_steps(p, first, last)]
    return (0 if first else bank_x_uses(g)) + (steps.index(("undo", k, False)) + 1)


def y_tiles(p):
    return slice(FC - n_tiles(p), FC) if p == 0 else slice(0, n_tiles(p))


def build(nc, ids, ctx, w, wt, w1, b1, w2, b2, w3, sel, selc, sel_undo, undo_rows, eyef, tables, out):
    with ExitStack() as stack:
        def sb(name, shape, dt):
            return stack.enter_context(nc.sbuf_tensor(name, shape, dt))

        def ps(name, shape, dt):
            return stack.enter_context(nc.psum_tensor(name, shape, dt))

        def sem(name):
            return stack.enter_context(nc.semaphore(name))

        s_parts = sb("s_parts", [P, TILES, P], F16)
        w_sum = sb("w_sum", [P, CU, P], F32)
        w_swapped = sb("w_swapped", [P, 2, SU, P], F32)
        s_h = sb("s_h", [P, 2, SU, P], F16)
        s_l = sb("s_l", [P, 2, SU, P], F16)
        w_max = sb("w_max", [P, SPLITS + 1], F32)
        w_max_all = sb("w_max_all", [1, 3], F32)
        ones = sb("ones", [1, P], F32)
        s_power = sb("s_power", [P, 1], F32)
        s_scale = sb("s_scale", [P, 1], F32)
        undo_rows_s = sb("undo_rows_s", [NS, 2], F32)
        undo_scale = sb("undo_scale", [NS, 1], F32)
        sel_undo_f = sb("sel_undo_f", [NS, NZ, P], F32)
        sel_undo_s = sb("sel_undo_s", [NS, NZ, P], BF16)
        x_max = sb("x_max", [P, 2, T], F32)
        x_power = sb("x_power", [P, T, NS], F32)
        x_scale = sb("x_scale", [P, 2, T], F32)
        powers_t = sb("powers_t", [NS, NB], BF16)
        undo = sb("undo", [P, 2, NB], F32)
        idx = sb("idx", [P, C, T * FC], I32)
        rows = sb("rows", [P, C, T, P + 1], F32)
        parts = sb("parts", [P, SLOTS, T, FC, PARTS, D], F16)
        x_stack = sb("x_stack", [P, F, NB], F16)
        x_chunk = sb("x_chunk", [P, SLOTS, NB], F32)
        prod = sb("prod", [P, 3, FC, NB], F32)
        z = sb("z", [P, NZ, NB], F32)
        z_heads = sb("z_heads", [P, HEADS, NB], F32)
        ctx_t = sb("ctx_t", [P, NB], F32)
        w1_s = sb("w1_s", [P, NZ, N1], F32)
        w2_s = sb("w2_s", [P, M1, N2], F32)
        w3_s = sb("w3_s", [P, M2], F32)
        b1_s = sb("b1_s", [P, M1], F32)
        b2_s = sb("b2_s", [P, M2], F32)
        h1 = sb("h1", [P, M1, NB], F32)
        h2 = sb("h2", [P, M2, NB], F32)
        y_s = sb("y_s", [1, NB], F32)
        sel_s = sb("sel_s", [P, UPB, D], F32)
        selc_s = sb("selc_s", [P, FC, D], F32)
        eye_f = sb("eye_f", [P, P], F32)
        eye_h = sb("eye_h", [P, P], F16)
        eye_b = sb("eye_b", [P, P], BF16)

        p_y = ps("p_y", [P, 2, FC, NB], F32)
        p_stack = ps("p_stack", [P, FC, NB], F16)
        p_x = ps("p_x", [P, 512], F32)
        p_d = ps("p_d", [P, 512], F32)
        p_z = ps("p_z", [P, 512], F32)

        ids_ready = [sem(f"ids_ready{c}") for c in range(C)]
        gathered = [sem(f"gathered{c}") for c in range(C)]
        chunk_begun = sem("chunk_begun")
        consts = sem("consts")
        mlp_weights = sem("mlp_weights")
        w_loaded = [sem(f"w_loaded{k}") for k in range(SPLITS)]
        wt_loaded = [sem(f"wt_loaded{k}") for k in range(SPLITS)]
        w_maxed, w_turned, w_power_known, s_power_out, s_scaled = (
            sem(n) for n in ("w_maxed", "w_turned", "w_power_known", "s_power_out", "s_scaled"))
        s_summed, s_high, s_low = (sem(n) for n in ("s_summed", "s_high", "s_low"))
        vector_step = sem("vector_step")
        s_placed = [sem(f"s_placed{k}") for k in range(SPLITS)]
        zeroed = sem("zeroed")
        eye_cast = sem("eye_cast")
        x_maxed, x_scaled, x_high, x_low, x_repeated = (
            sem(n) for n in ("x_maxed", "x_scaled", "x_high", "x_low", "x_repeated"))
        x_powered = sem("x_powered")
        turned, undo_made, undo_cast = (sem(n) for n in ("turned", "undo_made", "undo_cast"))
        transposed = sem("transposed")
        stack_ready = sem("stack_ready")
        bank_x_read = sem("bank_x_read")
        piece_read = sem("piece_read")
        y_ready = sem("y_ready")
        multiplied = sem("multiplied")
        reduced = sem("reduced")
        ctx_added = sem("ctx_added")
        z_copied = sem("z_copied")
        heads_moved = sem("heads_moved")
        ctx_loaded = sem("ctx_loaded")
        piece_done = sem("piece_done")
        y_stored = sem("y_stored")

        block = stack.enter_context(nc.Block())
        N_PLACED = 16 * PARTS * FC

        def gather_group(pool, g, first):
            for c in range(C):
                pool.wait_ge(ids_ready[c], g * 16 + 16)
                if not first:
                    pool.wait_ge(transposed, g * C + (c - C + 1))
                pool.sem_inc(chunk_begun, 1)
                for t in range(T):
                    for f in range(FC):
                        k = t * FC + f
                        pool.indirect_dma_start(
                            out=rows[:, c, t, f * D:(f + 1) * D], out_offset=None,
                            in_=tables[FC * c + f],
                            in_offset=bass.IndirectOffsetOnAxis(ap=idx[:, c, k:k + 1], axis=0),
                        ).then_inc(gathered[c], 16)

        N_GATHERED = 16 * T * FC

        @block.gpsimd
        def _(pool):
            gather_group(pool, 0, True)
            with pool.Fori(1, G) as g:
                gather_group(pool, g, False)

        @block.sync
        def _(sp):
            for c in range(C):
                sp.dma_start(idx[:, c, :], ids[:, 0, c, :]).then_inc(ids_ready[c], 16)

            def place(k):
                for q in range(FC):
                    for row, src in enumerate((s_h, s_h, s_l, s_l)):
                        tiles = s_parts[D * row:D * row + D, FC * SU * k:FC * SU * (k + 1), :]
                        sp.dma_start(tiles.rearrange("p (u q) n -> p u q n", q=FC)[:, :, q, :],
                                     src[D * q:D * q + D, k % 2, :, :]).then_inc(s_placed[k], 16)

            def load_swapped(k):
                sp.dma_start(w_swapped[:, k % 2, :, :], wt[:, k * SU:(k + 1) * SU, :]).then_inc(wt_loaded[k], 16)

            def reload_ids(g, c):
                sp.wait_ge(gathered[c], g * N_GATHERED + N_GATHERED)
                sp.dma_start(idx[:, c, :],
                             ids[:, bass.ds(g + 1, 1), c, :].rearrange("p a k -> p (a k)")).then_inc(ids_ready[c], 16)

            for k in range(SPLITS):
                sp.dma_start(w_sum[:, k * SU:(k + 1) * SU, :],
                             w[:, k * SU:(k + 1) * SU, :]).then_inc(w_loaded[k], 16)
            sp.dma_start(eye_f[:, :], eyef).then_inc(consts, 16)
            sp.dma_start(sel_s[:, :, :], sel).then_inc(consts, 16)
            sp.dma_start(selc_s[:, :, :], selc).then_inc(consts, 16)
            sp.dma_start(sel_undo_f[:, :, :], sel_undo).then_inc(consts, 16)
            sp.dma_start(undo_rows_s[:, :], undo_rows).then_inc(consts, 16)
            load_swapped(0)
            load_swapped(1)
            for k in range(SPLITS):
                if k == SPLITS - 1:
                    for c in range(C // 2):
                        reload_ids(0, c)
                sp.wait_ge(s_low, k + 1)
                place(k)
                if k + 2 < SPLITS:
                    load_swapped(k + 2)
            sp.dma_start(w1_s[:, :, :], w1).then_inc(mlp_weights, 16)
            sp.dma_start(w2_s[:, :, :], w2).then_inc(mlp_weights, 16)
            sp.dma_start(w3_s[:, :], w3).then_inc(mlp_weights, 16)
            sp.dma_start(b1_s[:, :], b1).then_inc(mlp_weights, 16)
            sp.dma_start(b2_s[:, :], b2).then_inc(mlp_weights, 16)
            for c in range(C // 2, C):
                reload_ids(0, c)

            with sp.Fori(1, G - 1) as g:
                for c in range(C):
                    reload_ids(g, c)

        steps = [0]

        def in_turn(v, instruction):
            steps[0] += 1
            instruction.then_inc(vector_step, 1)
            v.wait_ge(vector_step, steps[0])

        def s_scale_step(v):
            for k in range(SPLITS):
                v.wait_ge(w_loaded[k], 16)
                in_turn(v, nc.vector.tensor_reduce(w_max[:, k:k + 1],
                                                   w_sum[:, k * SU:(k + 1) * SU, :].rearrange("p t n -> p (t n)"),
                                                   AX.X, ALU.max, apply_absolute_value=True))
            nc.vector.tensor_reduce(w_max[:, SPLITS:SPLITS + 1], w_max[:, 0:SPLITS], AX.X,
                                    ALU.max).then_inc(w_maxed, 1)
            v.wait_ge(w_turned, 1)
            in_turn(v, nc.vector.tensor_reduce(w_max_all[:, 0:1], p_d[0:1, 0:P], AX.X, ALU.max))
            in_turn(v, nc.vector.tensor_scalar(w_max_all[:, 1:2], w_max_all[:, 0:1], TINY, None, ALU.max))
            nc.vector.tensor_scalar(w_max_all[:, 2:3].bitcast(I32), w_max_all[:, 1:2].bitcast(I32),
                                    EXPONENT, None, ALU.bitwise_and).then_inc(w_power_known, 1)
            v.wait_ge(s_power_out, 1)
            in_turn(v, nc.vector.tensor_copy(s_power[:, :], p_d[:, 256:257]))
            nc.vector.tensor_scalar(s_scale[:, :].bitcast(I32), s_power[:, :].bitcast(I32), -1.0,
                                    float((254 + S_EXP) << 23), ALU.mult, ALU.add).then_inc(s_scaled, 1)
            v.wait_ge(consts, 16 * 5)
            in_turn(v, nc.vector.scalar_tensor_tensor(undo_scale[:, :], undo_rows_s[:, 0:1], s_power[0:NS, 0:1],
                                                      undo_rows_s[:, 1:2], ALU.mult, ALU.add))
            nc.vector.tensor_scalar(sel_undo_s[:, :, :], sel_undo_f[:, :, :], undo_scale[:, 0:1], None,
                                    ALU.mult).then_inc(undo_cast, 1)

        def s_sum_step(v, k):
            piece = slice(k * SU, (k + 1) * SU)
            v.wait_ge(wt_loaded[k], 16)
            nc.vector.tensor_tensor(w_sum[:, piece, :], w_sum[:, piece, :], w_swapped[:, k % 2, :, :],
                                    ALU.add).then_inc(s_summed, 1)

        def s_low_step(v, k):
            piece = slice(k * SU, (k + 1) * SU)
            v.wait_ge(s_high, k + 1)
            if k >= 2:
                v.wait_ge(s_placed[k - 2], N_PLACED)
            nc.vector.scalar_tensor_tensor(
                s_l[:, k % 2, :, :].rearrange("p t n -> p (t n)"),
                w_sum[:, piece, :].rearrange("p t n -> p (t n)"), s_scale[:, 0:1],
                s_h[:, k % 2, :, :].rearrange("p t n -> p (t n)"), ALU.mult, ALU.subtract).then_inc(s_low, 1)

        def x_max_step(v, g, n, c, young):
            v.wait_ge(gathered[c], g * N_GATHERED + N_GATHERED)
            if not (young and c < 2):
                v.wait_ge(x_powered, n - 1)
            nc.vector.tensor_reduce(x_max[:, c % 2, :], rows[:, c, :, :], AX.X, ALU.max,
                                    apply_absolute_value=True).then_inc(x_maxed, 1)

        def x_power_step(v, n, c, turns):
            v.wait_ge(x_maxed, n + 1)
            if turns is not None:
                v.wait_ge(turned, turns)
            nc.vector.tensor_scalar(x_power[:, :, c].bitcast(I32), x_max[:, c % 2, :].bitcast(I32),
                                    EXPONENT, None, ALU.bitwise_and).then_inc(x_powered, 1)

        def x_scale_step(v, n, c, young):
            v.wait_ge(x_powered, n + 1)
            if not (young and c < 2):
                v.wait_ge(x_low, n - 1)
            nc.vector.tensor_scalar(x_scale[:, c % 2, :].bitcast(I32), x_power[:, :, c].bitcast(I32), -1.0,
                                    float((254 + X_EXP) << 23), ALU.mult, ALU.add).then_inc(x_scaled, 1)

        def x_low_step(v, n, c):
            v.wait_ge(x_high, n + 1)
            for t in range(T):
                last = nc.vector.scalar_tensor_tensor(
                    parts[:, c % SLOTS, t, :, 1, :], rows[:, c, t, 0:P].rearrange("p (f d) -> p f d", f=FC),
                    x_scale[:, c % 2, t:t + 1], parts[:, c % SLOTS, t, :, 0, :], ALU.mult, ALU.subtract)
            last.then_inc(x_low, 1)

        def z_out(v, g, k, young, last):
            v.wait_ge(bank_x_read, undo_use(g, k, young, last))
            if k < NZ - 1:
                v.wait_ge(reduced, g * NU + UPB * (k + 1))
            else:
                v.wait_ge(ctx_added, g + 1)
            if k == 0 and not young:
                v.wait_ge(heads_moved, g)
            if k == HEADS and not young:
                v.wait_ge(piece_done, g * PIECES - PIECES + M1)
            nc.vector.tensor_tensor(z_heads[:, k, :] if k < HEADS else z[:, k, :], p_z[:, 0:NB], undo[:, k % 2, :],
                                    ALU.mult).then_inc(z_copied, 1)

        def product(v, g, p, first):
            ci, cj = UNITS[p]
            nt = n_tiles(p)
            if ci == 0:
                v.wait_ge(stack_ready, g * C + (cj + 1))
            v.wait_ge(y_ready, g * NU + (p + 1))
            if p >= 3:
                v.wait_ge(reduced, g * NU + (p - 2))
            elif not first:
                v.wait_ge(reduced, g * NU + (p - 3))
            nc.vector.tensor_tensor(
                prod[:, p % 3, y_tiles(p), :], p_y[:, p % 2, y_tiles(p), :],
                x_chunk[:, cj % SLOTS, :].unsqueeze(1).broadcast_to([P, nt, NB]),
                ALU.mult).then_inc(multiplied, 1)

        def vector_position(v, g, p, first=False, last=False):
            def chunks(delay):
                return [(c, g + 1 if nxt else g, (g + 1 if nxt else g) * C + c, first and not nxt)
                        for c, nxt in chunks_at(p, MAX_AT, first, last, delay)]
            if first and p in S_SUM_AT:
                s_sum_step(v, S_SUM_AT[p])
            if first and p in S_LOW_AT:
                s_low_step(v, S_LOW_AT[p])
            for c, _gg, n, _young in chunks(L_DELAY):
                x_low_step(v, n, c)
            for c, _gg, n, young in chunks(H_DELAY):
                x_scale_step(v, n, c, young)
            for c, gg, n, young in chunks(0):
                x_max_step(v, gg, n, c, young)
            if p in Z_OUT_AT:
                z_out(v, g, Z_OUT_AT[p], first, last)
            if p == LATE and not first:
                z_out(v, g - 1, NZ - 1, False, False)
            if p >= 0:
                product(v, g, p, first)
            for c, _gg, n, _young in chunks(0):
                k = sum(at < p for at in TURN_AT)
                x_power_step(v, n, c, g * TURNS + k if k or not first else None)

        @block.vector
        def _(v):
            nc.vector.memset(ctx_t[:, :], 0.0).then_inc(zeroed, 1)
            nc.vector.memset(x_power[:, :, :], 1.0).then_inc(zeroed, 1)
            nc.vector.memset(ones[:, :], 1.0).then_inc(zeroed, 1)
            nc.vector.memset(rows[:, :, :, P:P + 1], TINY).then_inc(zeroed, 1)
            v.wait_ge(zeroed, 4)
            s_scale_step(v)
            for p in range(BEGIN, NU):
                vector_position(v, 0, p, first=True)
            with v.Fori(1, G - 1) as g:
                for p in range(NU):
                    vector_position(v, g, p)
            for p in range(NU):
                vector_position(v, G - 1, p, last=True)
            z_out(v, G - 1, NZ - 1, False, True)

        def s_high_step(a, k):
            a.wait_ge(s_summed, k + 1)
            if k == 0:
                a.wait_ge(s_scaled, 1)
            if k >= 2:
                a.wait_ge(s_placed[k - 2], N_PLACED)
            nc.scalar.activation(s_h[:, k % 2, :, :], w_sum[:, k * SU:(k + 1) * SU, :], ACT.Copy,
                                 scale=s_scale[:, 0:1]).then_inc(s_high, 1)

        def x_high_step(a, n, c, young):
            a.wait_ge(x_scaled, n + 1)
            if not (young and c < SLOTS):
                a.wait_ge(transposed, n - (SLOTS - 1))
            for t in range(T):
                last = nc.scalar.activation(parts[:, c % SLOTS, t, :, 0, :],
                                            rows[:, c, t, 0:P].rearrange("p (f d) -> p f d", f=FC),
                                            ACT.Copy, scale=x_scale[:, c % 2, t:t + 1])
            last.then_inc(x_high, 1)

        def repeat_parts(a, n, c):
            a.wait_ge(x_low, n + 1)
            pairs = parts[:, c % SLOTS, :, :, :, :].rearrange("p t f a d -> p (t f) (a d)")
            nc.scalar.activation(pairs[:, :, 2 * D:4 * D], pairs[:, :, 0:2 * D], ACT.Copy).then_inc(x_repeated, 1)

        def load_ctx(a, g):
            a.dma_start(ctx_t[0:NCTX, :], ctx[:, bass.ds(g * NB, NB)]).then_inc(ctx_loaded, 16)

        def transposed_out(a, g, n, c, young):
            a.wait_ge(transposed, n + 1)
            if c >= SLOTS:
                a.wait_ge(multiplied, g * NU + START[c - SLOTS + 1])
            elif not young:
                a.wait_ge(multiplied, g * NU - NU + START[c + C - SLOTS + 1])
            nc.scalar.activation(x_chunk[:, c % SLOTS, :], p_x[:, 0:NB], ACT.Copy).then_inc(bank_x_read, 1)
            if not young:
                a.wait_ge(y_ready, g * NU - NU + START[C - 1] + c + 1)
            nc.scalar.activation(x_stack[:, FC * c:FC * (c + 1), :], p_stack[:, :, :],
                                 ACT.Copy).then_inc(stack_ready, 1)

        def powers_out(a, g, k):
            a.wait_ge(turned, g * TURNS + (k + 1))
            nc.scalar.activation(powers_t[:, :], p_x[0:NS, 0:NB], ACT.Copy).then_inc(bank_x_read, 1)

        def undo_out(a, g, k, first):
            a.wait_ge(undo_made, g * NZ + (k + 1))
            if k >= 2:
                a.wait_ge(z_copied, g * NZ + (k - 1))
            elif not first:
                a.wait_ge(z_copied, g * NZ)
            nc.scalar.activation(undo[:, k % 2, :], p_x[:, 0:NB], ACT.Copy).then_inc(bank_x_read, 1)

        def piece_bank(i, tail):
            return (p_d, p_x)[i % 2] if tail else p_d

        def piece_out(a, g, i, tail=False):
            bank = piece_bank(i, tail)
            a.wait_ge(piece_done, g * PIECES + (i + 1))
            if i < M1:
                nc.scalar.activation(h1[:, i, :], bank[:, 0:NB], ACT.Relu,
                                     bias=b1_s[:, i:i + 1]).then_inc(piece_read, 1)
            elif i < M1 + M2:
                m = i - M1
                nc.scalar.activation(h2[:, m, :], bank[:, 0:NB], ACT.Relu,
                                     bias=b2_s[:, m:m + 1]).then_inc(piece_read, 1)
            else:
                nc.scalar.activation(y_s[:, :], bank[0:1, 0:NB], ACT.Copy).then_inc(piece_read, 1)
                a.wait_ge(piece_read, g * PIECES + PIECES)
                a.dma_start(out[:, bass.ds(g * NB, NB)], y_s[:, :]).then_inc(y_stored, 16)

        def scalar_position(a, g, p, first=False, last=False):
            if first and p in S_SUM_AT:
                s_high_step(a, S_SUM_AT[p])
            for kind, i, nxt in bank_x_steps(p, first, last):
                gg = g + 1 if nxt else g
                if kind == "chunk":
                    repeat_parts(a, gg * C + i, i)
                    transposed_out(a, gg, gg * C + i, i, first and not nxt)
                elif kind == "turn":
                    powers_out(a, g, i)
                elif kind == "undo":
                    undo_out(a, g, i, first)
            if p == HEADS_AT:
                a.wait_ge(z_copied, g * NZ + HEADS)
                if not first:
                    a.wait_ge(piece_done, g * PIECES - PIECES + M1)
                nc.scalar.activation(z[:, 0:HEADS, :], z_heads[:, :, :], ACT.Copy).then_inc(heads_moved, 1)
            if not first:
                if p in DENSE_AT and DENSE_AT[p][1] == dense_ks(DENSE_AT[p][0]) - 1:
                    piece_out(a, g - 1, DENSE_AT[p][0])
                if p == NU - 1:
                    a.wait_ge(y_stored, g * 16)
                if p == CTX_AT:
                    a.wait_ge(ctx_added, g)
                    load_ctx(a, g)
            for c, nxt in chunks_at(p, MAX_AT, first, last, H_DELAY):
                x_high_step(a, (g + 1) * C + c if nxt else g * C + c, c, first and not nxt)

        @block.scalar
        def _(a):
            a.wait_ge(zeroed, 4)
            load_ctx(a, 0)
            a.wait_ge(consts, 16 * 5)
            nc.scalar.activation(eye_b[:, :], eye_f[:, :], ACT.Copy).then_inc(eye_cast, 1)
            nc.scalar.activation(eye_h[:, :], eye_f[:, :], ACT.Copy).then_inc(eye_cast, 1)
            for p in range(BEGIN, NU):
                scalar_position(a, 0, p, first=True)
            a.wait_ge(mlp_weights, 16 * 5)
            with a.Fori(1, G - 1) as g:
                for p in range(NU):
                    scalar_position(a, g, p)
            for p in range(NU):
                scalar_position(a, G - 1, p, last=True)
            for i in range(PIECES):
                piece_out(a, G - 1, i, tail=True)
            a.wait_ge(y_stored, 16 * G)

        def transpose_chunk(t, n, c, bank_uses, young):
            t.wait_ge(x_repeated, n + 1)
            if not (young and c == 0):
                t.wait_ge(stack_ready, n)
                t.wait_ge(bank_x_read, bank_uses)
            for s in range(T):
                nc.tensor.transpose(p_x[:, s * P:(s + 1) * P], rows[:, c, s, 0:P], eye_f[:, :])
            for s in range(T):
                for f in range(FC):
                    last = nc.tensor.transpose(p_stack[:, f, s * P:(s + 1) * P],
                                               parts[:, c % SLOTS, s, f, :, :].rearrange("p a d -> p (a d)"),
                                               eye_h[:, :])
            last.then_inc(transposed, 1)

        def turn_powers(t, g, p, bank_uses, last_group):
            done = sum(at < p for at in MAX_AT)
            early = 0 if last_group else sum(at + NU < p for at in MAX_AT)
            t.wait_ge(x_powered, g * C + (done + early))
            t.wait_ge(bank_x_read, bank_uses)
            for s in range(T):
                power = x_power[:, s, :].bitcast(BF16)[:, 1:2 * NS:2]
                last = nc.tensor.matmul(p_x[0:NS, s * P:(s + 1) * P], power, eye_b[:, :], start=True, stop=True)
            last.then_inc(turned, 1)

        def lay_out_undo(t, k, bank_uses):
            t.wait_ge(bank_x_read, bank_uses)
            nc.tensor.matmul(p_x[:, 0:NB], sel_undo_s[:, k, :], powers_t[:, :],
                             start=True, stop=True).then_inc(undo_made, 1)

        def interact(t, g, p, first):
            ci, cj = UNITS[p]
            if ci == 0:
                t.wait_ge(stack_ready, g * C + (cj + 1))
            if first and (p == 0 or split_of(p) > max(split_of(u) for u in range(p))):
                t.wait_ge(s_placed[split_of(p)], N_PLACED)
            if p >= 2:
                t.wait_ge(multiplied, g * NU + (p - 1))
            elif not first:
                t.wait_ge(multiplied, g * NU + (p - 2))
            for q in range(n_tiles(p)):
                tile, y = tile_of(p, q), y_tiles(p).start + q
                if ci != cj:
                    x_i = x_stack[:, FC * ci + q, :]
                    last = nc.tensor.matmul(p_y[:, p % 2, y, :], s_parts[:, tile, :], x_i,
                                            start=True, stop=True)
                else:
                    for s in range(FC):
                        x_i = x_stack[:, fields_of(p, q, s)[0], :]
                        last = nc.tensor.matmul(p_y[D * s:D * s + D, p % 2, y, :],
                                                s_parts[:, tile, D * s:D * s + D], x_i, start=True, stop=True)
            last.then_inc(y_ready, 1)

        def reduce(t, g, p, first):
            k, m = p // UPB, p % UPB
            if m == 0 and not (k == 0 and first):
                t.wait_ge(z_copied, g * NZ + k)
            t.wait_ge(multiplied, g * NU + (p + 1))
            for q in range(n_tiles(p)):
                begin = not any(n_tiles(u) > q for u in range(UPB * k, p))
                end = k < NZ - 1 and not any(n_tiles(u) > q for u in range(p + 1, UPB * (k + 1)))
                last = nc.tensor.matmul(p_z[D * q:D * q + D, 0:NB], sel_s[:, m, :],
                                        prod[:, p % 3, y_tiles(p).start + q, :], start=begin, stop=end)
            last.then_inc(reduced, 1)

        def add_ctx(t, g):
            t.wait_ge(ctx_loaded, g * 16 + 16)
            for q in range(FC):
                last = nc.tensor.matmul(p_z[D * q:D * q + D, 0:NB], selc_s[:, q, :], ctx_t[:, :],
                                        start=False, stop=True)
            last.then_inc(ctx_added, 1)

        def dense_product(t, g, i, k, tail=False):
            if tail:
                if i == 0 and k == 0:
                    t.wait_ge(heads_moved, g + 1)
                elif i == 0 and k >= HEADS:
                    t.wait_ge(z_copied, g * NZ + (k + 1))
                elif i >= 2 and k == 0:
                    t.wait_ge(piece_read, g * PIECES + (i - 1))
                if M1 <= i < M1 + M2:
                    t.wait_ge(piece_read, g * PIECES + (k + 1))
                elif i == M1 + M2:
                    t.wait_ge(piece_read, g * PIECES + (M1 + k + 1))
            elif (i, k) == (0, 0):
                t.wait_ge(z_copied, g * NZ + NZ)
                t.wait_ge(heads_moved, g + 1)
            elif k == 0:
                t.wait_ge(piece_read, g * PIECES + i)
            begin, end = k == 0, k == dense_ks(i) - 1
            bank = piece_bank(i, tail)
            if i < M1:
                last = nc.tensor.matmul(bank[:, 0:NB], w1_s[:, k, i * P:(i + 1) * P], z[:, k, :],
                                        start=begin, stop=end)
            elif i < M1 + M2:
                m = i - M1
                last = nc.tensor.matmul(bank[:, 0:NB], w2_s[:, k, m * P:(m + 1) * P], h1[:, k, :],
                                        start=begin, stop=end)
            else:
                last = nc.tensor.matmul(bank[0:1, 0:NB], w3_s[:, k:k + 1], h2[:, k, :], start=begin, stop=end)
            if end:
                last.then_inc(piece_done, 1)

        def tensor_group(t, g, first=False, last=False):
            uses = sum(at < 0 for at in TRANSPOSE_AT_FIRST) if first else bank_x_uses(g)
            for p in range(NU):
                interact(t, g, p, first)
                for kind, i, nxt in bank_x_steps(p, first, last):
                    if kind == "chunk":
                        transpose_chunk(t, (g + 1) * C + i if nxt else g * C + i, i, uses, False)
                    elif kind == "turn":
                        turn_powers(t, g, p, uses, last)
                    elif kind == "undo":
                        lay_out_undo(t, i, uses)
                    uses = uses + 1
                if not first:
                    if p in DENSE_AT:
                        dense_product(t, g - 1, *DENSE_AT[p])
                    if p == Y_READ_AT:
                        t.wait_ge(piece_read, g * PIECES)
                if last and p >= TAIL_AT:
                    dense_product(t, g, 0, p - TAIL_AT, tail=True)
                if p >= LATE:
                    reduce(t, g, p - LATE, first)
                elif not first:
                    reduce(t, g - 1, p - LATE + NU, False)
                    if p == LATE - 1:
                        add_ctx(t, g - 1)

        @block.tensor
        def _(t):
            t.wait_ge(consts, 16 * 5)
            t.wait_ge(w_maxed, 1)
            nc.tensor.matmul(p_d[0:1, 0:P], w_max[:, SPLITS:SPLITS + 1], eye_f[:, :],
                             start=True, stop=True).then_inc(w_turned, 1)
            t.wait_ge(w_power_known, 1)
            nc.tensor.matmul(p_d[:, 256:257], ones[:, :], w_max_all[:, 2:3],
                             start=True, stop=True).then_inc(s_power_out, 1)
            t.wait_ge(eye_cast, 2)
            t.wait_ge(undo_cast, 1)
            uses = 0
            for p in range(BEGIN, 0):
                for _kind, c, _nxt in bank_x_steps(p, first=True):
                    transpose_chunk(t, c, c, uses, True)
                    uses += 1
            tensor_group(t, 0, first=True)
            t.wait_ge(mlp_weights, 16 * 5)
            with t.Fori(1, G - 1) as g:
                tensor_group(t, g)
            tensor_group(t, G - 1, last=True)
            for k in range(NU - TAIL_AT, NZ - 1):
                dense_product(t, G - 1, 0, k, tail=True)
            for u in range(NU - LATE, NU):
                reduce(t, G - 1, u, False)
            add_ctx(t, G - 1)
            t.wait_ge(bank_x_read, bank_x_uses(G - 1) + sum(len(bank_x_steps(p, last=True)) for p in range(NU)))
            for k in range(NZ - 1):
                dense_product(t, G - 1, 1, k, tail=True)
            for i in range(PIECES):
                for k in range(NZ - 1 if i < 2 else 0, dense_ks(i)):
                    dense_product(t, G - 1, i, k, tail=True)


def _layouts():
    pair_of = {}
    for i in range(F):
        for j in range(i + 1, F):
            pair_of[i, j] = pair_of[j, i] = len(pair_of) // 2
    tile_pairs = np.zeros((TILES, FC), np.int64)
    z_pair = np.full(NZ * P, -1, np.int64)
    seen = set()
    for u in range(NU):
        for q in range(n_tiles(u)):
            for s in range(FC):
                pair = pair_of[fields_of(u, q, s)]
                tile_pairs[tile_of(u, q), s] = pair
                if pair not in seen:
                    seen.add(pair)
                    z_pair[(u // UPB) * P + D * q + FC * (u % UPB) + s] = pair
    for r in range(NCTX):
        z_pair[(NU // UPB) * P + D * (r // FC) + FC * (NU % UPB) + r % FC] = F * (F - 1) // 2 + r
    sel = np.zeros((P, UPB, D), np.float32)
    for s in range(FC):
        for m in range(UPB):
            sel[D * s:D * s + D, m, FC * m + s] = 1
    selc = np.zeros((P, FC, D), np.float32)
    for r in range(NCTX):
        selc[r, r // FC, FC * (NU % UPB) + r % FC] = 1
    sel_undo = np.zeros((NS, NZ, P), np.float32)
    for u in range(NU):
        for q in range(FC):
            first = D * q + FC * (u % UPB)
            sel_undo[UNITS[u][0], u // UPB, first:first + FC] = 1
            sel_undo[C, NU // UPB, D * q + FC * (NU % UPB):D * q + FC * (NU % UPB) + FC] = 1
    undo_rows = np.zeros((NS, 2), np.float32)
    undo_rows[:C, 0] = 2.0 ** -(X_EXP + S_EXP)
    undo_rows[C:, 1] = 1
    return tile_pairs, z_pair, sel, selc, sel_undo, undo_rows


def kernel(**inputs):
    import concourse.bacc as bacc
    from concourse.bass_utils import run_bass_kernel_spmd

    tile_pairs, z_pair, sel, selc, sel_undo, undo_rows = _layouts()
    a = {k: np.asarray(v) for k, v in inputs.items()}
    ids = a["ids"].reshape(G, T, P, C, FC).transpose(2, 0, 3, 1, 4).reshape(P, G, C, T * FC)
    w = a["L0_rec_W"][tile_pairs]
    w = w.reshape(CU, FC, FC, D, D)
    w1 = np.zeros((NZ * P, N1), np.float32)
    w1[z_pair >= 0] = a["W_top1"][z_pair[z_pair >= 0]]
    arrays = {
        "ids_in": ids,
        "ctx_in": a["dense_ctx"].T,
        "w_in": w.transpose(1, 3, 0, 2, 4).reshape(P, CU, P),
        "wt_in": w.transpose(1, 4, 0, 2, 3).reshape(P, CU, P),
        "w1_in": w1.reshape(NZ, P, N1).transpose(1, 0, 2),
        "b1_in": a["b_top1"].reshape(M1, P).T,
        "w2_in": a["W_top2"].reshape(M1, P, N2).transpose(1, 0, 2),
        "b2_in": a["b_top2"].reshape(M2, P).T,
        "w3_in": a["W_top3"].reshape(M2, P).T,
        "sel_in": sel,
        "selc_in": selc,
        "sel_undo_in": sel_undo,
        "undo_rows_in": undo_rows,
        "eye_in": np.eye(P, dtype=np.float32),
    }
    tables = {f"table{f}_in": a[f"tbl_{f}"] for f in range(F)}
    arrays = {k: np.ascontiguousarray(v) for k, v in {**arrays, **tables}.items()}
    nc = bacc.Bacc("TRN2", target_bir_lowering=False, num_devices=1)
    aps = {k: nc.dram_tensor(k, v.shape, mybir.dt.from_np(v.dtype), kind="ExternalInput").ap()
           for k, v in arrays.items()}
    out = nc.dram_tensor("y_out", (1, B), F32, kind="ExternalOutput").ap()
    build(nc, aps["ids_in"], aps["ctx_in"], aps["w_in"], aps["wt_in"], aps["w1_in"], aps["b1_in"],
          aps["w2_in"], aps["b2_in"], aps["w3_in"], aps["sel_in"], aps["selc_in"], aps["sel_undo_in"],
          aps["undo_rows_in"], aps["eye_in"],
          [aps[f"table{f}_in"] for f in range(F)], out)
    r = run_bass_kernel_spmd(nc, [arrays], core_ids=[0])
    return r.results[0]["y_out"].reshape(B, 1)
```
